# Optimizing a Trainium2 kernel written in Bass

```python
import numpy as np
import jax
import jax.numpy as jnp

def _softmax(x, axis=-1):
    return jax.nn.softmax(x, axis=axis)

def _gelu(x):
    return jax.nn.gelu(x, approximate=True)

def _silu(x):
    return jax.nn.silu(x)

def _sigmoid(x):
    return jax.nn.sigmoid(x)

def _layernorm(x, axis=-1, eps=1e-05):
    m = jnp.mean(x, axis=axis, keepdims=True)
    v = jnp.var(x, axis=axis, keepdims=True)
    return (x - m) / jnp.sqrt(v + eps)

def _scatter_add(tgt, idx, src, axis=0):
    return tgt.at[idx].add(src)

def _segment_sum(src, seg, n):
    return jax.ops.segment_sum(src, seg, n)
kernel_name = 'mk_vit_tower_cls_d1_tok_img4096_r4_7762e8'

def setup_inputs(seed: int=0):
    np.random.seed(seed)
    _w = jnp.asarray

    def _rec_inputs():
        import jax
        import jax.numpy as jnp
        _rk = jax.random.key(seed)
        x = -0.0064186 + 0.999588 * jax.random.normal(jax.random.fold_in(_rk, 1), (32, 128, 64, 2), jnp.float32)
        cls_tok = 0.02 * jax.random.normal(jax.random.fold_in(_rk, 5), (1, 1, 1024), jnp.float32)
        return (x, cls_tok)
    x, cls_tok = _rec_inputs()

    def _L0_tok_setup():
        import jax, jax.numpy as jnp
        import numpy as np
        import math
        H, N, C, L_VAL = (128, 64, 1, 1024)
        EPS = 1e-07

        def _reciprocal(x, epsilon):
            xc = jnp.conj(x)
            return xc / (x * xc + epsilon)
        key = jax.random.key(seed)
        k1, k2, k3 = jax.random.split(key, 3)
        log_dt = math.log(0.001) + jax.random.uniform(k1, (H,), dtype=jnp.float32) * (math.log(0.1) - math.log(0.001))
        log_dt = jnp.tile(log_dt[:, None], (1, 2))
        lam_im = jax.random.normal(k2, (N,), dtype=jnp.float32)
        Lambda = jnp.stack([-0.5 * jnp.ones((N,), jnp.float32), lam_im], axis=-1)
        W = jax.random.normal(k3, (C, H, N, 2), dtype=jnp.float32)
        return {'log_dt': log_dt, 'Lambda': Lambda, 'W': W, 'L': L_VAL}
    _L0_tok_all = _L0_tok_setup()
    _L0_tok_in = {k: v for k, v in _L0_tok_all.items() if k in ('log_dt', 'Lambda')}
    del _L0_tok_all

    def _L0_attn_setup():
        import jax, jax.numpy as jnp
        import numpy as np
        import math
        HIDDEN = 1024
        N_HEADS = 32
        N_KV_HEADS = 8
        HEAD_DIM = HIDDEN // N_HEADS
        GROUPS = N_HEADS // N_KV_HEADS
        ROPE_THETA = 10000.0
        TOKEN_BUDGET = 128
        INIT_BUDGET = 128
        RECENT_BUDGET = 128
        CHUNK = 16
        B, S = (1, 512)

        def _rotate_half(x):
            x1, x2 = jnp.split(x, 2, axis=-1)
            return jnp.concatenate([-x2, x1], axis=-1)

        def _rope(seq_len, dtype):
            inv_freq = 1.0 / ROPE_THETA ** (jnp.arange(0, HEAD_DIM, 2, dtype=jnp.float32) / HEAD_DIM)
            freqs = jnp.arange(seq_len, dtype=jnp.float32)[:, None] * inv_freq[None, :]
            emb = jnp.concatenate([freqs, freqs], axis=-1)
            return (jnp.cos(emb).astype(dtype), jnp.sin(emb).astype(dtype))
        key = jax.random.key(seed)
        ks = jax.random.split(key, 5)
        sc = 0.02
        return {'hidden_states': jax.random.normal(ks[0], (B, S, HIDDEN), dtype=jnp.float32), 'wq': jax.random.normal(ks[1], (N_HEADS * HEAD_DIM, HIDDEN), dtype=jnp.float32) * sc, 'wk': jax.random.normal(ks[2], (N_KV_HEADS * HEAD_DIM, HIDDEN), dtype=jnp.float32) * sc, 'wv': jax.random.normal(ks[3], (N_KV_HEADS * HEAD_DIM, HIDDEN), dtype=jnp.float32) * sc, 'wo': jax.random.normal(ks[4], (HIDDEN, N_HEADS * HEAD_DIM), dtype=jnp.float32) * sc}
    _L0_attn_all = _L0_attn_setup()
    _L0_attn_in = {k: v for k, v in _L0_attn_all.items() if k in ('wq', 'wk', 'wv', 'wo')}
    del _L0_attn_all

    def _L0_ffn_setup():
        import jax, jax.numpy as jnp
        import numpy as np
        K, OUT, IN = (4, 1024, 1024)
        key = jax.random.key(seed)
        k1, k2, k3 = jax.random.split(key, 3)
        x = jax.random.normal(k1, (4, 512, IN), dtype=jnp.float32)
        bits = jax.random.randint(k2, (K, OUT, IN), 0, 2)
        bases = (2 * bits - 1).astype(jnp.int8)
        alphas = jax.random.uniform(k3, (K, OUT, 1), dtype=jnp.float32)
        return {'x': x, 'bases': bases, 'alphas': alphas}
    _L0_ffn_all = _L0_ffn_setup()
    _L0_ffn_in = {k: v for k, v in _L0_ffn_all.items() if k in ('bases', 'alphas')}
    del _L0_ffn_all
    return {'x': x, 'cls_tok': cls_tok, 'L0_tok_log_dt': _L0_tok_in['log_dt'], 'L0_tok_Lambda': _L0_tok_in['Lambda'], 'L0_attn_wq': _L0_attn_in['wq'], 'L0_attn_wk': _L0_attn_in['wk'], 'L0_attn_wv': _L0_attn_in['wv'], 'L0_attn_wo': _L0_attn_in['wo'], 'L0_ffn_bases': _L0_ffn_in['bases'], 'L0_ffn_alphas': _L0_ffn_in['alphas']}

def reference(x, cls_tok, L0_tok_log_dt, L0_tok_Lambda, L0_attn_wq, L0_attn_wk, L0_attn_wv, L0_attn_wo, L0_ffn_bases, L0_ffn_alphas):
    import jax
    import jax.numpy as jnp

    def _L0_tok_ref(log_dt, Lambda, W, L):
        import jax, jax.numpy as jnp
        import numpy as np
        import math
        H, N, C, L_VAL = (128, 64, 1, 1024)
        EPS = 1e-07

        def _reciprocal(x, epsilon):
            xc = jnp.conj(x)
            return xc / (x * xc + epsilon)
        Lam = Lambda[:, 0] + 1j * Lambda[:, 1]
        Wc = W[..., 0] + 1j * W[..., 1]
        dt = jnp.exp(log_dt)
        dt_Lambda = dt[:, None, 0] * Lambda[None, :, 0] + 1j * (dt[:, None, 1] * Lambda[None, :, 1])
        pos = jnp.arange(L, dtype=jnp.float32)
        gt0 = (Lam.real > 0).astype(dt_Lambda.real.dtype)
        P_max = jax.lax.stop_gradient(dt_Lambda * (gt0 * (L - 1)))
        dt_Lambda_neg = dt_Lambda * (1 - 2 * gt0)
        num = jnp.exp(dt_Lambda_neg) - 1
        den = jnp.exp(dt_Lambda_neg * L) - 1
        Wc = Wc * num * _reciprocal(den * Lam, EPS)
        P = dt_Lambda[..., None] * pos - P_max[..., None]
        K = jnp.einsum('chn,hnl->chl', Wc, jnp.exp(P))
        return K.real.astype(jnp.float32)

    def _L0_attn_ref(hidden_states, wq, wk, wv, wo):
        import jax, jax.numpy as jnp
        import numpy as np
        import math
        HIDDEN = 1024
        N_HEADS = 32
        N_KV_HEADS = 8
        HEAD_DIM = HIDDEN // N_HEADS
        GROUPS = N_HEADS // N_KV_HEADS
        ROPE_THETA = 10000.0
        TOKEN_BUDGET = 128
        INIT_BUDGET = 128
        RECENT_BUDGET = 128
        CHUNK = 16
        B, S = (1, 512)

        def _rotate_half(x):
            x1, x2 = jnp.split(x, 2, axis=-1)
            return jnp.concatenate([-x2, x1], axis=-1)

        def _rope(seq_len, dtype):
            inv_freq = 1.0 / ROPE_THETA ** (jnp.arange(0, HEAD_DIM, 2, dtype=jnp.float32) / HEAD_DIM)
            freqs = jnp.arange(seq_len, dtype=jnp.float32)[:, None] * inv_freq[None, :]
            emb = jnp.concatenate([freqs, freqs], axis=-1)
            return (jnp.cos(emb).astype(dtype), jnp.sin(emb).astype(dtype))
        b, s, _ = hidden_states.shape
        dtype = hidden_states.dtype
        NEG = jnp.finfo(dtype).min
        q = (hidden_states @ wq.T).reshape(b, s, N_HEADS, HEAD_DIM).transpose(0, 2, 1, 3)
        k = (hidden_states @ wk.T).reshape(b, s, N_KV_HEADS, HEAD_DIM).transpose(0, 2, 1, 3)
        v = (hidden_states @ wv.T).reshape(b, s, N_KV_HEADS, HEAD_DIM).transpose(0, 2, 1, 3)
        cos, sin = _rope(s, dtype)
        q = q * cos[None, None] + _rotate_half(q) * sin[None, None]
        k = k * cos[None, None] + _rotate_half(k) * sin[None, None]
        k = jnp.repeat(k, GROUPS, axis=1)
        v = jnp.repeat(v, GROUPS, axis=1)
        scores = jnp.einsum('bhqd,bhkd->bhqk', q, k) / math.sqrt(HEAD_DIM)
        q_pos = jnp.arange(s)[:, None]
        k_pos = jnp.arange(s)[None, :]
        causal = k_pos <= q_pos
        masked = jnp.where(causal[None, None], scores, NEG)
        pad = -s % CHUNK
        padded = jnp.pad(masked, ((0, 0), (0, 0), (0, 0), (0, pad)), constant_values=NEG)
        n_chunks = (s + pad) // CHUNK
        chunk_max = padded.reshape(b, N_HEADS, s, n_chunks, CHUNK).max(axis=-1)
        k_top = min(max(3, TOKEN_BUDGET // CHUNK), n_chunks)
        _, topk_idx = jax.lax.top_k(chunk_max, k_top)
        chunk_mask = jnp.any(topk_idx[..., None] == jnp.arange(n_chunks), axis=-2)
        tok_mask = jnp.repeat(chunk_mask, CHUNK, axis=-1)[..., :s]
        init_mask = k_pos < INIT_BUDGET
        recent_mask = k_pos > q_pos - RECENT_BUDGET
        allowed = causal[None, None] & (tok_mask | init_mask[None, None] | recent_mask[None, None])
        final = jnp.where(allowed, scores, NEG)
        attn = jax.nn.softmax(final, axis=-1)
        out = jnp.einsum('bhqk,bhkd->bhqd', attn, v)
        out = out.transpose(0, 2, 1, 3).reshape(b, s, N_HEADS * HEAD_DIM)
        return out @ wo.T

    def _L0_ffn_ref(x, bases, alphas):
        import jax, jax.numpy as jnp
        import numpy as np
        K, OUT, IN = (4, 1024, 1024)
        W_q = jnp.sum(alphas * bases.astype(x.dtype), axis=0)
        return jnp.einsum('bsi,oi->bso', x, W_q)
    h = _L0_tok_ref(L0_tok_log_dt, L0_tok_Lambda, x, 1024)
    h = jnp.concatenate([jnp.broadcast_to(cls_tok, (h.shape[0], 1, h.shape[2])), h], axis=1)
    h = h + _L0_attn_ref(_layernorm(h, axis=-1), L0_attn_wq, L0_attn_wk, L0_attn_wv, L0_attn_wo)
    h = h + _L0_ffn_ref(_layernorm(h, axis=-1), L0_ffn_bases, L0_ffn_alphas)
    return h

_drawn_inputs = setup_inputs


def setup_inputs(seed=0):
    import zlib

    import numpy as np

    out = dict(_drawn_inputs(seed))
    spreads = {}
    factors = {}
    for name, (base, spread) in spreads.items():
        noise = np.random.default_rng([zlib.crc32(name.encode()), seed]).standard_normal(out[name].shape)
        drawn = base * np.exp(spread * noise) if base else spread * noise
        out[name] = jnp.asarray(drawn.astype(out[name].dtype))
    for name, factor in factors.items():
        out[name] = (out[name] * factor).astype(out[name].dtype)
    return out
```

```python
import math
from contextlib import ExitStack

import numpy as np

import concourse.bass as bass
from concourse import mybir

F32 = mybir.dt.float32
F32R = mybir.dt.float32r
BF16 = mybir.dt.bfloat16
I8 = mybir.dt.int8
ALU = mybir.AluOpType
ACT = mybir.ActivationFunctionType
AX = mybir.AxisListType

P = 128
NB = 32
T = 128
D = 1024
NS = 64
IC = D // P
HD = 32
GROUPS = 4
KVW = 256
QKV = D + 2 * KVW
NA, NBT = 4, 256
NC, ND = 16, 16
EPS_TOK = 1e-7
EPS_LN = 1e-5
TWO_PI = 2.0 * math.pi
MAGIC = 1.5 * 2.0**23
TURN = 6.283185
NEG = -1.0e30


def host_constants():
    half = np.arange(P) // NS
    c = {}
    e = np.concatenate([ND * np.arange(NC), np.arange(ND), NBT * np.arange(NA)])
    c["exps"] = np.tile(e.astype(np.float32), (P, 1))
    top = [0.25, 0, 0.25, 0.5, 0.25, 0, -1]
    bot = [0, 0.25, -0.25, 0.5, 0.25, 0, 1]
    c["shifts"] = np.array([top if x == 0 else bot for x in half], np.float32)
    c["ident"] = np.eye(P, dtype=np.float32)
    q, k = np.arange(T)[:, None], np.arange(T)[None, :]
    c["mask"] = np.where(k <= q, 0.0, NEG).astype(np.float32)
    inv = 1.0 / 10000.0 ** (np.arange(0, HD, 2, dtype=np.float32) / HD)
    f = np.arange(T + 1, dtype=np.float32)[:, None] * inv[None, :].astype(np.float32)
    emb = np.concatenate([f, f], axis=-1)[1:]
    cos, sin = np.cos(emb).T, np.sin(emb).T
    sin = np.concatenate([-sin[: HD // 2], sin[HD // 2:]])
    c["rope"] = np.concatenate([np.tile(cos, (4, 1)), np.tile(sin, (4, 1))], axis=1).astype(np.float32)
    return c


def need(engine, semaphore, value):
    if not (isinstance(value, int) and value <= 0):
        engine.wait_ge(semaphore, value)


def hold(engine, passed):
    engine.sem_inc(passed, 1)


def position_tables(nc, mem, io):
    OB = D // P
    NK = 4
    NP = 3
    with ExitStack() as ctx:
        sb = lambda n, s, d=F32: ctx.enter_context(nc.sbuf_tensor(n, s, d))
        sem = lambda n: ctx.enter_context(nc.semaphore(n))
        H = P
        logdt = sb("logdt", [P, 2, H])
        dt = sb("dt", [P, 2, H])
        lam = sb("lam", [P, 2])
        exps = sb("t_exps", [P, NC + ND + NA])
        eshift = sb("eshift", [P, NC + ND + NA])
        shifts = sb("t_shifts", [P, 7])
        g = sb("g", [P, 4])
        a = sb("a", [P, 2, H])
        turns = sb("turns", [P, H])
        z = sb("z", [P, 2, 2, H])
        trig = mem["trig"]
        whole = sb("whole", [P, 4096])
        mag = sb("mag", [P, 2 * 2048 + 512])
        em = sb("em", [P, 2, H])
        tmp = [sb(f"tmp{i}", [P, 2, H]) for i in range(4)]
        nd_re = sb("nd_re", [P, 2, H])
        nd_im = sb("nd_im", [P, 2, H])
        y = sb("y", [P, 2, H])
        y2 = sb("y2", [P, 3, H])
        F = sb("F", [P, 2, H])
        identf = sb("t_ident", [P, P])
        identb = sb("t_identb", [P, P], BF16)
        alpha = [sb(f"alpha{i}", [P, OB * NK]) for i in range(NP)]
        alpha_part = sb("alpha_part", [P, OB * NK, NP], BF16)
        base8 = [sb(f"base8_{i}", [P, NK, D], I8) for i in range(2)]
        base16 = [sb(f"base16_{i}", [P, NK, D], BF16) for i in range(2)]
        diag = [sb(f"diag{i}", [P, NK * NP, P], BF16) for i in range(2)]
        wf_parts = [[sb(f"wf_part{i}_{k}", [P, IC // 2, P], F32R) for k in range(2)] for i in range(2)]
        wo_in = [sb(f"wo_in{i}", [P, D]) for i in range(2)]
        wo_parts = [[sb(f"wo_part{i}_{k}", [P, D], F32R) for k in range(2)] for i in range(2)]
        pW = [ctx.enter_context(nc.psum_tensor(f"t_pW{i}", [P, IC // 2, P], F32)) for i in range(4)]
        loaded = sem("t_loaded")
        alpha_loaded = sem("t_alpha_loaded")
        base_loaded = [sem(f"t_base_loaded{i}") for i in range(2)]
        wo_loaded = [sem(f"t_wo_loaded{i}") for i in range(2)]
        cast = sem("t_cast")
        diag_ready = sem("t_diag_ready")
        wf_ready = sem("t_wf_ready")
        wf_high = sem("t_wf_high")
        wf_low = sem("t_wf_low")
        wo_high = sem("t_wo_high")
        wo_low = sem("t_wo_low")
        wf_stored = [sem(f"t_wf_stored{i}") for i in range(2)]
        wo_stored = [sem(f"t_wo_stored{i}") for i in range(2)]
        dt_ready = sem("t_dt_ready")
        a_ready = sem("t_a_ready")
        mag_in = sem("t_mag_in_ready")
        mag_ready = sem("t_mag_ready")
        z_ready = sem("t_z_ready")
        tanh_ready = sem("t_tanh_ready")
        phase_ready = sem("t_phase_ready")
        sin_ready = sem("t_sin_ready")
        pool_chain = sem("t_pool_chain")
        chain = sem("t_vector_chain")
        block = ctx.enter_context(nc.Block())

        segs = mem["segs"]
        seg = lambda n: trig[:, segs[n][0]:segs[n][0] + segs[n][1]]
        spans = [(segs["Ar"][0], segs["end"][0]), (segs["D1"][0], segs["Ar"][0]), (0, segs["D1"][0])]
        outer_of = lambda v, e0, ne: (v.unsqueeze(2).broadcast_to([P, H, ne]),
                                      eshift[:, e0:e0 + ne].unsqueeze(1).broadcast_to([P, H, ne]))
        grid = lambda v, ne: v.rearrange("p (h e) -> p h e", e=ne)

        @block.sync
        def _(sp):
            sp.dma_start(logdt[:], io["log_dt"].partition_broadcast(P)).then_inc(loaded, 16)
            for half in range(2):
                sp.dma_start(lam[NS * half:NS * half + NS, :], io["Lambda"]).then_inc(loaded, 16)
            sp.dma_start(exps[:], io["exps"]).then_inc(loaded, 16)
            sp.dma_start(shifts[:], io["shifts"]).then_inc(loaded, 16)
            sp.dma_start(alpha[0][:], io["alphas"]).then_inc(alpha_loaded, 16)
            sp.dma_start(identf[:], io["ident"]).then_inc(alpha_loaded, 16)

            def load_wo(n):
                need(sp, wo_low, n - 1)
                sp.dma_start(wo_in[n % 2][:], io["wo"][:, n, :]).then_inc(wo_loaded[n % 2], 16)

            for n in range(2):
                sp.dma_start(base8[n][:], io["bases"][:, n]).then_inc(base_loaded[n], 16)
            for n in range(2):
                load_wo(n)
            def store_parts(n):
                for q in range(2):
                    sp.wait_ge(wf_low, 2 * n + q + 1)
                    for k, name in enumerate(("wfh", "wfl")):
                        dst = io[name][:, 4 * q:4 * q + 4, n * P:(n + 1) * P]
                        sp.dma_start(dst, wf_parts[q][k][:].bitcast(F32)).then_inc(wf_stored[q], 16)

            for n in range(OB):
                sp.wait_ge(wo_low, n + 1)
                for k, name in enumerate(("woh", "wol")):
                    sp.dma_start(io[name][:, n, :], wo_parts[n % 2][k][:].bitcast(F32)).then_inc(wo_stored[n % 2], 16)
                if n + 2 < OB:
                    load_wo(n + 2)
                store_parts(n)
                if n < 2:
                    half = slice(NS * n, NS * n + NS)
                    other = slice(NS * (1 - n), NS * (1 - n) + NS)
                    sp.dma_start(mem["w1"][half], io["W"][half]).then_inc(mem["w_loaded"], 16)
                    sp.dma_start(mem["w2"][half], io["W"][other]).then_inc(mem["w_loaded"], 16)
            for i in range(2):
                sp.wait_ge(wo_stored[i], 16 * OB)
                sp.wait_ge(wf_stored[i], 32 * OB)

        @block.tensor
        def _(pe):
            def step(n, i, u):
                pe.wait_ge(cast, n + 1)
                pe.wait_ge(diag_ready, n + 1)
                for q in range(2):
                    need(pe, wf_low, 2 * n + q - 3)
                    for c in range(IC // 2):
                        col = (IC // 2 * q + c) * P
                        for k in range(NK):
                            for part in range(NP):
                                last = nc.tensor.matmul(pW[2 * u + q][:, c, :], base16[u][:, k, col:col + P],
                                                        diag[u][:, NP * k + part, :],
                                                        start=(k + part == 0), stop=(k == NK - 1 and part == NP - 1))
                    last.then_inc(wf_ready, 1)

            for u in range(2):
                step(u, 0, u)
            with pe.Fori(1, OB // 2) as i:
                for u in range(2):
                    step(2 * i + u, i, u)

        @block.gpsimd
        def _(pool):
            n = [0]

            def link(ins):
                n[0] += 1
                ins.then_inc(pool_chain, 1)
                pool.wait_ge(pool_chain, n[0])

            G_ = nc.gpsimd
            pool.wait_ge(alpha_loaded, 32)
            link(G_.tensor_copy(identb[:], identf[:]))
            for part in range(NP):
                link(G_.tensor_copy(alpha_part[:, :, part], alpha[part][:]))
                if part + 1 < NP:
                    link(G_.tensor_tensor(alpha[part + 1][:], alpha[part][:], alpha_part[:, :, part], ALU.subtract))

            def diagonal(b):
                need(pool, wf_ready, 2 * (b - 1))
                v = alpha_part[:, NK * b:NK * (b + 1), :].rearrange("p k r -> p (k r)")
                nc.gpsimd.tensor_tensor(diag[b % 2][:], identb[:].unsqueeze(1).broadcast_to([P, NK * NP, P]),
                                        v.unsqueeze(2).broadcast_to([P, NK * NP, P]), ALU.mult).then_inc(diag_ready, 1)

            def wo_lower(c):
                pool.wait_ge(wo_high, c + 1)
                G_.tensor_tensor(wo_parts[c % 2][1][:], wo_in[c % 2][:], wo_parts[c % 2][0][:].bitcast(F32),
                                 ALU.subtract).then_inc(wo_low, 1)

            diagonal(0)
            diagonal(1)
            pool.wait_ge(a_ready, 1)
            for k, (lo, e0, ne) in enumerate(((2048, NC, ND), (0, 0, NC), (4096, NC + ND, NA))):
                last = G_.tensor_tensor(grid(mag[:, lo:lo + H * ne], ne), *outer_of(a[:, 0, :], e0, ne), ALU.mult)
            last.then_inc(mag_in, 1)
            for b in range(2, OB):
                wo_lower(b - 2)
                diagonal(b)
            for c in range(OB - 2, OB):
                wo_lower(c)

        @block.scalar
        def _(act):
            act.wait_ge(loaded, 80)
            nc.scalar.activation(dt[:], logdt[:], ACT.Exp).then_inc(dt_ready, 1)

            def cast_base(b):
                act.wait_ge(base_loaded[b % 2], 16 * (b // 2 + 1))
                need(act, wf_ready, 2 * (b - 1))
                nc.scalar.activation(base16[b % 2][:], base8[b % 2][:], ACT.Copy).then_inc(cast, 1)

            def load_base(b):
                act.wait_ge(cast, b - 1)
                act.dma_start(base8[b % 2][:], io["bases"][:, b]).then_inc(base_loaded[b % 2], 16)

            def wo_upper(c):
                act.wait_ge(wo_loaded[c % 2], 16 * (c // 2 + 1))
                if c >= 2:
                    act.wait_ge(wo_stored[c % 2], 32 * (c // 2))
                nc.scalar.activation(wo_parts[c % 2][0][:], wo_in[c % 2][:], ACT.Copy).then_inc(wo_high, 1)

            def wf_upper(b):
                for q in range(2):
                    act.wait_ge(wf_ready, 2 * b + q + 1)
                    if b >= 1:
                        act.wait_ge(wf_stored[q], 32 * b)
                    nc.scalar.activation(wf_parts[q][0][:], pW[2 * (b % 2) + q][:], ACT.Copy).then_inc(wf_high, 1)

            cast_base(0)
            load_base(2)
            cast_base(1)
            wo_upper(0)
            load_base(3)
            act.wait_ge(z_ready, 1)
            nc.scalar.activation(em[:], z[:, :, 0, :], ACT.Tanh, scale=0.5).then_inc(tanh_ready, 1)
            for b in range(OB):
                wf_upper(b)
                if b + 2 < OB:
                    cast_base(b + 2)
                if b == 0:
                    act.wait_ge(mag_in, 1)
                    nc.scalar.activation(mag[:], mag[:], ACT.Exp).then_inc(mag_ready, 1)
                if b < 3:
                    lo, hi = spans[b]
                    act.wait_ge(phase_ready, b + 1)
                    nc.scalar.activation(trig[:, lo:hi], trig[:, lo:hi], ACT.Sin, scale=TURN).then_inc(sin_ready, 1)
                if b + 1 < OB:
                    wo_upper(b + 1)
                if b + 4 < OB:
                    load_base(b + 4)

        @block.vector
        def _(dve):
            n = [0]

            def link(ins):
                n[0] += 1
                ins.then_inc(chain, 1)
                dve.wait_ge(chain, n[0])

            V = nc.vector

            def wf_lower(*blocks):
                for b in blocks:
                    for q in range(2):
                        dve.wait_ge(wf_high, 2 * b + q + 1)
                        V.tensor_tensor(wf_parts[q][1][:], pW[2 * (b % 2) + q][:], wf_parts[q][0][:].bitcast(F32),
                                        ALU.subtract).then_inc(wf_low, 1)

            dve.wait_ge(loaded, 80)
            link(V.tensor_scalar(g[:, 0:1], lam[:, 0:1], 0.0, None, ALU.is_gt))
            V.tensor_scalar(g[:, 1:2], g[:, 0:1], -float(NBT - 1), None, ALU.mult)
            V.tensor_scalar(g[:, 2:3], g[:, 0:1], -float(NBT * (NA - 1)), None, ALU.mult)
            link(V.tensor_scalar(g[:, 3:4], g[:, 0:1], -2.0, 1.0, ALU.mult, ALU.add))
            V.tensor_scalar(eshift[:, 0:NC], exps[:, 0:NC], g[:, 1:2], None, ALU.add)
            V.tensor_copy(eshift[:, NC:NC + ND], exps[:, NC:NC + ND])
            link(V.tensor_scalar(eshift[:, NC + ND:], exps[:, NC + ND:], g[:, 2:3], None, ALU.add))
            dve.wait_ge(dt_ready, 1)
            for i in range(2):
                link(V.tensor_scalar(a[:, i, :], dt[:, i, :], lam[:, i:i + 1], None, ALU.mult))
            link(V.tensor_scalar(turns[:], a[:, 1, :], 1.0 / TWO_PI, None, ALU.mult))
            V.tensor_scalar(z[:, 0], a[:], g[:, 3:4], None, ALU.mult).then_inc(a_ready, 1)
            dve.wait_ge(a_ready, 1)
            V.tensor_scalar(z[:, 1], z[:, 0], float(D), None, ALU.mult).then_inc(z_ready, 1)
            dve.wait_ge(z_ready, 1)
            yy = seg("Y").rearrange("p (s r h) -> p s r h", s=2, r=2)
            V.tensor_scalar(yy[:, 0], z[:, :, 1, :], 1.0 / TWO_PI, None, ALU.mult)
            link(V.tensor_scalar(yy[:, 1], z[:, :, 1, :], 0.5 / TWO_PI, None, ALU.mult))

            def phases(i, base, e0, ne, others):
                link(V.tensor_tensor(grid(seg(base), ne), *outer_of(turns[:], e0, ne), ALU.mult))
                for name, k in others:
                    link(V.tensor_scalar(seg(name), seg(base), shifts[:, k:k + 1], None, ALU.add))
                lo, hi = spans[i]
                x, k = trig[:, lo:hi], whole[:, 0:hi - lo]
                link(V.tensor_scalar(k, x, MAGIC, MAGIC, ALU.add, ALU.subtract))
                V.tensor_tensor(x, x, k, ALU.subtract).then_inc(phase_ready, 1)
                dve.wait_ge(phase_ready, i + 1)

            phases(0, "Ai", NC + ND, NA, [("Ar", 4)])
            phases(1, "D1", NC, ND, [("D2", 3), ("D1", 2)])
            wf_lower(0)
            phases(2, "C1", 0, NC, [("C2", 1), ("C1", 0)])
            wf_lower(1)
            wf_lower(2)
            dve.wait_ge(tanh_ready, 1)
            link(V.tensor_scalar(tmp[1][:], em[:], -1.0, 1.0, ALU.mult, ALU.add))
            link(V.reciprocal(tmp[1][:], tmp[1][:]))
            link(V.scalar_tensor_tensor(em[:], em[:], 2.0, tmp[1][:], ALU.mult, ALU.mult))
            dve.wait_ge(sin_ready, 1)
            link(V.tensor_tensor(tmp[1][:], yy[:, 1], yy[:, 1], ALU.mult))
            link(V.tensor_scalar(tmp[2][:], em[:], 1.0, None, ALU.add))
            link(V.tensor_tensor(nd_im[:], tmp[2][:], yy[:, 0], ALU.mult))
            link(V.tensor_tensor(tmp[1][:], tmp[1][:], tmp[2][:], ALU.mult))
            link(V.scalar_tensor_tensor(nd_re[:], tmp[1][:], -2.0, em[:], ALU.mult, ALU.add))
            link(V.tensor_scalar(tmp[3][:, 0], nd_im[:, 1], lam[:, 1:2], None, ALU.mult))
            link(V.scalar_tensor_tensor(y[:, 0], nd_re[:, 1], lam[:, 0:1], tmp[3][:, 0], ALU.mult, ALU.subtract))
            link(V.tensor_scalar(tmp[3][:, 1], nd_im[:, 1], lam[:, 0:1], None, ALU.mult))
            link(V.scalar_tensor_tensor(y[:, 1], nd_re[:, 1], lam[:, 1:2], tmp[3][:, 1], ALU.mult, ALU.add))
            link(V.tensor_tensor(y2[:, 0:2], y[:], y[:], ALU.mult))
            link(V.scalar_tensor_tensor(y2[:, 2], y2[:, 0], EPS_TOK, y2[:, 1], ALU.add, ALU.add))
            link(V.reciprocal(y2[:, 2], y2[:, 2]))
            wf_lower(3)
            link(V.tensor_tensor(tmp[1][:, 0], nd_re[:, 0], y[:, 0], ALU.mult))
            link(V.tensor_tensor(tmp[1][:, 1], nd_im[:, 0], y[:, 0], ALU.mult))
            link(V.tensor_tensor(tmp[2][:, 0], nd_im[:, 0], y[:, 1], ALU.mult))
            link(V.tensor_tensor(tmp[2][:, 1], nd_re[:, 0], y[:, 1], ALU.mult))
            link(V.tensor_tensor(tmp[1][:, 0], tmp[1][:, 0], tmp[2][:, 0], ALU.add))
            link(V.tensor_tensor(tmp[1][:, 1], tmp[1][:, 1], tmp[2][:, 1], ALU.subtract))
            link(V.tensor_tensor(F[:], tmp[1][:], y2[:, 2:3].broadcast_to([P, 2, H]), ALU.mult))
            dve.wait_ge(mag_ready, 1)
            for name in ("Ar", "Ai"):
                link(V.tensor_tensor(seg(name), seg(name), mag[:, 4096:4608], ALU.mult))
            Ar, Ai = (grid(seg(s), NA) for s in ("Ar", "Ai"))
            Fr, Fi = (F[:, i, :].unsqueeze(2).broadcast_to([P, H, NA]) for i in range(2))
            t0, t1 = (grid(whole[:, 512 * i:512 * i + 512], NA) for i in range(2))
            FA1, FA2 = (grid(mem["FA"][:, i], NA) for i in range(2))
            link(V.tensor_tensor(t0, Fr, Ar, ALU.mult))
            link(V.tensor_tensor(t1, Fi, Ai, ALU.mult))
            link(V.tensor_tensor(FA1, t0, t1, ALU.subtract))
            link(V.tensor_tensor(t0, Fr, Ai, ALU.mult))
            link(V.tensor_tensor(t1, Fi, Ar, ALU.mult))
            link(V.tensor_tensor(t0, t0, t1, ALU.add))
            link(V.tensor_scalar(FA2, t0, shifts[:, 6:7], None, ALU.mult))
            wf_lower(4)
            dve.wait_ge(sin_ready, 2)
            for name in ("D1", "D2"):
                V.tensor_tensor(seg(name), seg(name), mag[:, 2048:4096], ALU.mult)
            dve.wait_ge(sin_ready, 3)
            for name in ("C1", "C2"):
                V.tensor_tensor(seg(name), seg(name), mag[:, 0:2048], ALU.mult)
            wf_lower(5, 6, 7)


def token_kernels(nc, mem, io):
    HC = 4
    CH = P // HC
    PIECE = QKV * IC // CH
    NBUF = 2
    with ExitStack() as ctx:
        sb = lambda n, s, d=F32: ctx.enter_context(nc.sbuf_tensor(n, s, d))
        sem = lambda n: ctx.enter_context(nc.semaphore(n))
        w1, w2 = mem["w1"], mem["w2"]
        B = [sb(f"B{i}", [P, HC * NBT]) for i in range(NBUF)]
        B2 = [sb(f"B2_{i}", [P, HC * NBT]) for i in range(NBUF)]
        G = [sb(f"G{i}", [P, HC * NA * NB]) for i in range(NBUF)]
        G2 = [sb(f"G2_{i}", [P, HC * NA * NB]) for i in range(NBUF)]
        xk = [sb(f"xk{i}", [P, HC * NBT]) for i in range(NBUF)]
        wst = [sb(f"wst{i}", [P, PIECE]) for i in range(NBUF)]
        ps = [ctx.enter_context(nc.psum_tensor(f"kps{i}", [P, HC * NBT], F32)) for i in range(NBUF)]
        w_loaded = mem["w_loaded"]
        b1 = sem("k_b1")
        b2 = sem("k_b2")
        g1 = sem("k_g1")
        g2 = sem("k_g2")
        g_ready = sem("k_g_ready")
        multiplied = sem("k_multiplied")
        evicted = sem("k_evicted")
        stored = [sem(f"k_stored{i}") for i in range(NBUF)]
        piece_loaded = [sem(f"k_piece_loaded{i}") for i in range(NBUF)]
        hi_ready = sem("k_hi_ready")
        lo_ready = sem("k_lo_ready")
        block = ctx.enter_context(nc.Block())
        trig, segs = mem["trig"], mem["segs"]

        def chunk(view, i, n):
            return view.rearrange("p (c q) -> p c q", c=CH)[:, bass.ds(i, 1), :].rearrange(
                "p o (h e) -> p (o h) e", e=n)

        def table(name, i, n):
            return chunk(trig[:, segs[name][0]:segs[name][0] + segs[name][1]], i, n)

        def b_product(C, D):
            return (C.unsqueeze(3).broadcast_to([P, HC, NC, ND]), D.unsqueeze(2).broadcast_to([P, HC, NC, ND]))

        def g_product(W, F):
            return (W.unsqueeze(2).broadcast_to([P, HC, NA, NB]), F.unsqueeze(3).broadcast_to([P, HC, NA, NB]))

        b_view = lambda ap: ap.rearrange("p (h c d) -> p h c d", h=HC, c=NC)
        g_view = lambda ap: ap.rearrange("p (h a c) -> p h a c", h=HC, a=NA)
        piece = lambda w, i: w.rearrange("p (c q) -> p c q", c=CH)[:, bass.ds(i, 1), :].rearrange("p o q -> p (o q)")

        def chunks(engine, step, tail=1):
            for u in range(NBUF):
                step(u, u, 0)
            with engine.Fori(1, CH // NBUF - tail) as j:
                for u in range(NBUF):
                    step(NBUF * j + u, u, j)
            for i in range(CH - NBUF * tail, CH):
                step(i, i % NBUF, i // NBUF)

        def load_piece(engine, i, u):
            src = io["wqkv"][:, bass.ds(i, 1), :].rearrange("p o q -> p (o q)")
            engine.dma_start(wst[u][:], src).then_inc(piece_loaded[u], 16)

        @block.sync
        def _(sp):
            for u in range(NBUF):
                load_piece(sp, u, u)

            def step(i, u, j):
                sp.wait_ge(evicted, i + 1)
                for a in range(NA):
                    dst = io["x_tok"][0:NB, bass.ds(i * HC, HC), NBT * a:NBT * (a + 1)]
                    src = xk[u][NB * a:NB * (a + 1), :].rearrange("c (h b) -> c h b", h=HC)
                    sp.dma_start(dst, src).then_inc(stored[u], 16)

            chunks(sp, step)
            for u in range(NBUF):
                sp.wait_ge(stored[u], 16 * NA * CH // NBUF)

        @block.gpsimd
        def _(pool):
            pool.wait_ge(w_loaded, 64)

            def step(i, u, j):
                need(pool, multiplied, i - 1)
                nc.gpsimd.tensor_tensor(b_view(B2[u][:]), *b_product(table("C2", i, NC), table("D2", i, ND)),
                                        ALU.mult).then_inc(b2, 1)
                nc.gpsimd.tensor_tensor(g_view(G2[u][:]), *g_product(chunk(w2[:], i, NB), chunk(mem["FA"][:, 1], i, NA)),
                                        ALU.mult).then_inc(g2, 1)

            chunks(pool, step)

        @block.vector
        def _(dve):
            dve.wait_ge(w_loaded, 64)

            def step(i, u, j):
                need(dve, multiplied, i - 1)
                nc.vector.tensor_tensor(b_view(B[u][:]), *b_product(table("C1", i, NC), table("D1", i, ND)),
                                        ALU.mult).then_inc(b1, 1)
                nc.vector.tensor_tensor(g_view(G[u][:]), *g_product(chunk(w1[:], i, NB), chunk(mem["FA"][:, 0], i, NA)),
                                        ALU.mult).then_inc(g1, 1)
                dve.wait_ge(hi_ready, i + 1)
                nc.vector.tensor_tensor(piece(mem["wl"], i), wst[u][:], piece(mem["wh"], i).bitcast(F32),
                                        ALU.subtract).then_inc(lo_ready, 1)
                dve.wait_ge(g1, i + 1)
                dve.wait_ge(g2, i + 1)
                nc.vector.tensor_tensor(G[u][:], G[u][:], G2[u][:], ALU.add).then_inc(g_ready, 1)

            chunks(dve, step)

        @block.tensor
        def _(pe):
            def step(i, u, j):
                pe.wait_ge(b1, i + 1)
                pe.wait_ge(b2, i + 1)
                pe.wait_ge(g_ready, i + 1)
                need(pe, evicted, i - 1)
                for h in range(HC):
                    cols = slice(h * NBT, (h + 1) * NBT)
                    for k, b in enumerate((B, B2)):
                        last = nc.tensor.matmul(ps[u][:, cols], G[u][:, h * P:(h + 1) * P], b[u][:, cols],
                                                start=(k == 0), stop=(k == 1))
                last.then_inc(multiplied, 1)

            chunks(pe, step)

        @block.scalar
        def _(act):
            def upper(i, u, loads):
                act.wait_ge(piece_loaded[u], 16 * loads)
                nc.scalar.activation(piece(mem["wh"], i), wst[u][:], ACT.Copy).then_inc(hi_ready, 1)

            def load_next(i, u):
                act.wait_ge(lo_ready, i - 1)
                load_piece(act, i, u)

            upper(0, 0, 1)
            load_next(2, 0)

            def step(i, u, j):
                if not (isinstance(i, int) and i + 1 >= CH):
                    upper(i + 1, 1 - u, j + u + 1)
                act.wait_ge(multiplied, i + 1)
                need(act, stored[u], 16 * NA * j)
                nc.scalar.activation(xk[u][:], ps[u][:], ACT.Copy).then_inc(evicted, 1)
                if not (isinstance(i, int) and i + 3 >= CH):
                    load_next(i + 3, 1 - u)

            chunks(act, step, tail=2)


def attention(nc, mem, io):
    PAIRS = NB // 2
    W2 = 2 * T
    SCALE = 1.0 / math.sqrt(HD)
    ITEMS = [
        [("q", 0), ("x", 0, 0), ("q", 1), ("x", 0, 1), ("k", 0)],
        [("q", 2), ("x", 0, 2), ("q", 3), ("x", 0, 3), ("k", 1)],
        [("v", 0), ("x", 1, 0), ("q", 4), ("x", 1, 1), ("q", 5)],
        [("v", 1), ("x", 1, 2), ("q", 6), ("x", 1, 3), ("q", 7)],
    ]
    FIRST = ([("x", -1, q) for q in range(4)] + [("cv",), ("ck",), ("cvt",)]
             + [("x", b, q) for b in range(2) for q in range(4)]
             + [i for slot in ITEMS for i in slot if i[0] != "x"]
             + [("x", b, q) for b in range(2, 4) for q in range(4)])
    NFIRST = len(FIRST)
    assert NFIRST % 2 == 1
    PER_STEP = 20
    LAG = 4

    with ExitStack() as ctx:
        sb = lambda n, s, d=F32: ctx.enter_context(nc.sbuf_tensor(n, s, d))
        sem = lambda n: ctx.enter_context(nc.semaphore(n))
        wh, wl = (mem[k].rearrange("p (i n) -> p i n", i=IC) for k in ("wh", "wl"))
        ident = sb("a_ident", [P, P])
        mask = sb("a_mask", [P, T])
        rope = sb("a_rope", [P, 2, T])
        xt = [sb(f"a_x{i}", [P, D]) for i in range(2)]
        xn = sb("a_xn", [P, D])
        stats = sb("a_stats", [P, 2, 6])
        mv = sb("a_mv", [P, 2])
        rstd = sb("a_rstd", [P, 1])
        minus_half = sb("a_minus_half", [P, 1])
        xh = [sb(f"a_xh{i}", [P, IC, W2], F32R) for i in range(2)]
        xl = [sb(f"a_xl{i}", [P, IC, W2], F32R) for i in range(2)]
        QT = [sb(f"a_QT{i}", [P, IC, W2]) for i in range(2)]
        KT = [sb(f"a_KT{i}", [P, 2, W2]) for i in range(2)]
        V = [sb(f"a_V{i}", [P, 2, KVW]) for i in range(2)]
        rc = [sb(f"a_rc{i}", [P, W2]) for i in range(2)]
        rs = [sb(f"a_rs{i}", [P, W2]) for i in range(2)]
        pr = [sb(f"a_pr{i}", [P, 16 * T]) for i in range(2)]
        pt = [sb(f"a_pt{i}", [P, 4 * T]) for i in range(2)]
        ob = [sb(f"a_ob{i}", [P, 4 * T]) for i in range(2)]
        mx = [sb(f"a_mx{i}", [P, 16]) for i in range(2)]
        nm = [sb(f"a_nm{i}", [P, 16]) for i in range(2)]
        sums = [sb(f"a_sums{i}", [P, 16]) for i in range(2)]
        ecls = [sb(f"a_ecls{i}", [P, 16]) for i in range(2)]
        rec = [sb(f"a_rec{i}", [P, 16]) for i in range(2)]
        kcls = sb("a_kcls", [P, 2])
        vcol = sb("a_vcol", [P, 2])
        vrow = sb("a_vrow", [P, KVW])
        pS = [ctx.enter_context(nc.psum_tensor(f"a_pS{j}", [P, 4 * T], F32)) for j in range(4)]
        pT = ctx.enter_context(nc.psum_tensor("a_pT", [P, 4 * T], F32))
        pO = ctx.enter_context(nc.psum_tensor("a_pO", [P, 4 * T], F32))
        pI = [ctx.enter_context(nc.psum_tensor(f"a_pI{j}", [P, 2 * W2], F32))[:, 0:W2] for j in range(2)]

        const_loaded = sem("a_const_loaded")
        x_loaded = [sem(f"a_x_loaded{i}") for i in range(2)]
        cls_stored = sem("a_cls_stored")
        o_stored = [sem(f"a_o_stored{i}") for i in range(2)]
        half_ready = sem("a_half_ready")
        stats_ready = sem("a_stats_ready")
        mv_ready = sem("a_mv_ready")
        var_eps = sem("a_var_eps_ready")
        rstd_ready = sem("a_rstd_ready")
        xn_ready = sem("a_xn_ready")
        item_ready = sem("a_item_ready")
        item_taken = sem("a_item_taken")
        high_ready = sem("a_high_ready")
        key_ready = sem("a_key_ready")
        sin_done = sem("a_sin_done")
        roped = sem("a_roped")
        scored = sem("a_scored")
        masked = sem("a_masked")
        maxed = sem("a_maxed")
        bias_ready = sem("a_bias_ready")
        exped = sem("a_exped")
        ecls_ready = sem("a_ecls_ready")
        summed = sem("a_summed")
        rec_ready = sem("a_rec_ready")
        normed = sem("a_normed")
        pt_ready = sem("a_pt_ready")
        pt_copied = sem("a_pt_copied")
        pv_done = sem("a_pv_done")
        o_ready = sem("a_o_ready")
        passed_vector = sem("a_passed_vector")
        passed_pool = sem("a_passed_pool")
        block = ctx.enter_context(nc.Block())

        def item_list(t, brings_next=True, brings_rows=True):
            out, n = [], 0
            base = NFIRST + PER_STEP * t
            for u, slot in enumerate(ITEMS):
                for k, item in enumerate(slot):
                    if (item[0] == "x" and brings_rows) or (item[0] != "x" and brings_next):
                        out.append((u, k, item, base + n, (NFIRST + n) % 2))
                        n += 1
            return out

        def slot_items(its, u, *positions):
            return [(item, g, half) for (v, k, item, g, half) in its if v == u and k in positions]

        def steps(engine, step):
            for t in range(2):
                step(t, t, True, True, True)
            with engine.Fori(1, PAIRS // 2 - 2) as i:
                for par in range(2):
                    step(2 * i + par, par, True, True, True)
            for t in range(PAIRS - 4, PAIRS):
                step(t, t % 2, t + 1 < PAIRS, t + 2 < PAIRS, t + 2 < PAIRS)
            step(PAIRS, 0, False, False, False)

        def norms_batch(t, u):
            return 2 * t + u // 2 + LAG + 1

        exists = lambda b: not isinstance(b, int) or b < NB
        is_unit = lambda s: not isinstance(s, int) or 0 <= s < 4 * PAIRS

        def earlier(t, u, n):
            return (t, u - n) if u >= n else (t - 1, u - n + 4)

        @block.sync
        def _(sp):
            sp.dma_start(xt[1][:], io["cls"].partition_broadcast(P)).then_inc(x_loaded[1], 16)
            sp.dma_start(xt[0][:], io["x_tok"][0]).then_inc(x_loaded[0], 16)
            for buf, name in ((ident[:], "ident"), (mask[:], "mask"), (rope[:], "rope")):
                sp.dma_start(buf, io[name]).then_inc(const_loaded, 16)
            sp.wait_ge(x_loaded[1], 16)
            sp.dma_start(io["x_tok"][NB], xt[1][:]).then_inc(cls_stored, 16)

            def load_x(b, par, waits=True):
                if isinstance(b, int) and b == 1:
                    sp.wait_ge(cls_stored, 16)
                sp.wait_ge(xn_ready, b)
                src = io["x_tok"][bass.ds(b, 1)].rearrange("o t d -> (o t) d")
                sp.dma_start(xt[par][:], src).then_inc(x_loaded[par], 16)

            for b in range(1, LAG + 2):
                load_x(b, b % 2)
            for kb in range(2):
                sp.wait_ge(o_ready, kb + 1)
                sp.dma_start(io["attn"][NB, :, 512 * kb:512 * kb + 512], ob[kb][:]).then_inc(o_stored[kb], 16)

            def load_parts():
                sp.wait_ge(item_ready, NFIRST + PER_STEP * (PAIRS - 2) + PER_STEP - 8)
                for name in ("woh", "wol", "wfh"):
                    dst = mem[name].rearrange("p (i n) -> p i n", i=IC).bitcast(F32)
                    sp.dma_start(dst, io[name]).then_inc(mem["parts_loaded"], 16)

            def step(t, par, nxt, rows, norm):
                if isinstance(t, int) and t == PAIRS - 1:
                    load_parts()
                for u in range(4):
                    s = 4 * t + u
                    if is_unit(s - 3):
                        store(s - 3, *earlier(t, u, 3))
                    if u % 2 == 1 and norm:
                        b = norms_batch(t, u) + 1
                        if exists(b):
                            load_x(b, (u // 2 + LAG + 2) % 2)

            def store(s, t, u):
                sp.wait_ge(o_ready, s + 3)
                b = 2 * t + u // 2
                dst = io["attn"][bass.ds(b, 1), :, 512 * (u % 2):512 * (u % 2) + 512].rearrange("o p n -> (o p) n")
                sp.dma_start(dst, ob[u % 2][:]).then_inc(o_stored[u % 2], 16)

            steps(sp, step)
            for i in range(2):
                sp.wait_ge(o_stored[i], 16 * (2 * PAIRS + 1))

        @block.gpsimd
        def _(pool):
            nc.gpsimd.memset(minus_half[:], -0.5).then_inc(half_ready, 1)
            pool.wait_ge(half_ready, 1)
            pool.wait_ge(const_loaded, 48)

            def root(n):
                pool.wait_ge(var_eps, n + 1)
                nc.gpsimd.tensor_tensor(rstd[:], mv[:, 1:2], minus_half[:], ALU.pow).then_inc(rstd_ready, 1)

            def rotate(item, g, pair, r, par, buf):
                if item[0] == "q":
                    pool.wait_ge(item_taken, g + 1)
                else:
                    pool.wait_ge(key_ready, 2 * pair + item[1] + 1)
                out = QT[par][:, item[1], :] if item[0] == "q" else KT[par][:, item[1], :]
                both = lambda ap: ap.rearrange("p (b t) -> p b t", b=2)
                sin = rope[:, 1:2, :].broadcast_to([P, 2, T])
                nc.gpsimd.tensor_tensor(both(rs[buf][:]), both(rs[buf][:]), sin, ALU.mult).then_inc(sin_done, 1)
                pool.wait_ge(sin_done, r + 1)
                nc.gpsimd.tensor_tensor(out, rc[buf][:], rs[buf][:], ALU.add).then_inc(roped, 1)

            def normalize(s, par):
                pool.wait_ge(rec_ready, s + 1)
                hold(pool, passed_pool)
                for j in range(4):
                    for m in range(4):
                        i = 4 * j + m
                        v = pr[par][:, i * T:(i + 1) * T]
                        last = nc.gpsimd.tensor_scalar(v, v, rec[par][:, i:i + 1], 1.0, ALU.mult, ALU.mult)
                    last.then_inc(normed, 1)

            for n in range(4):
                root(n)
            r = 0
            for g, item in enumerate(FIRST):
                if item[0] in "qk":
                    rotate(item, g, 0, r, 0, r % 2)
                    r += 1
            for n in range(4, LAG + 2):
                root(n)

            def step(t, par, nxt, rows, norm):
                its = item_list(t, nxt, rows)
                r = 0
                for u in range(4):
                    for k in range(0, 5, 2):
                        if k == 4 and is_unit(4 * t + u - 1):
                            normalize(4 * t + u - 1, (u + 1) % 2)
                        for item, g, half in slot_items(its, u, k):
                            if item[0] in "qk":
                                rotate(item, g, t + 1, 10 * (t + 1) + r, 1 - par, r % 2)
                                r += 1
                    if u % 2 == 0 and norm and exists(norms_batch(t, u)):
                        root(norms_batch(t, u) + 1)

            steps(pool, step)

        @block.scalar
        def _(act):
            def high(item, g, half, par):
                act.wait_ge(item_ready, g + 1)
                b, q = max(item[1], 0) % 2, item[2]
                nc.scalar.activation(xh[par][:, 2 * q:2 * q + 2, b * T:(b + 1) * T],
                                     pI[half].rearrange("p (i t) -> p i t", i=2), ACT.Copy).then_inc(high_ready, 1)

            def exponentials(s, j, par):
                act.wait_ge(bias_ready, 4 * s + j + 1)
                for m in range(4):
                    i = 4 * j + m
                    v = pr[par][:, i * T:(i + 1) * T]
                    last = nc.scalar.activation(v, v, ACT.Exp, bias=nm[par][:, i:i + 1], scale=SCALE,
                                                accum_out=sums[par][:, i:i + 1])
                last.then_inc(exped, 1)

            def copy_pt(s, j):
                act.wait_ge(pt_ready, 4 * s + j + 1)
                need(act, pv_done, 4 * s + j - 1)
                nc.scalar.activation(pt[j % 2][:], pT[:], ACT.Copy).then_inc(pt_copied, 1)

            for g, item in enumerate(FIRST):
                if item[0] == "x":
                    high(item, g, g % 2, 1 if item[1] < 0 or item[1] > 1 else 0)

            def step(t, par, nxt, rows, norm):
                its = item_list(t, nxt, rows)
                for u in range(4):
                    s = 4 * t + u
                    soft = lambda *js: [exponentials(s - 1, j, (u + 1) % 2) for j in js if is_unit(s - 1)]
                    copies = lambda *js: [copy_pt(s - 2, j) for j in js if is_unit(s - 2)]
                    highs = lambda k: [high(item, g, half, par) for item, g, half in slot_items(its, u, k)]
                    soft(0, 1)
                    highs(1)
                    copies(0)
                    soft(2)
                    copies(1)
                    soft(3)
                    if is_unit(s - 1):
                        nc.scalar.activation(ecls[(u + 1) % 2][:], nm[(u + 1) % 2][:], ACT.Exp).then_inc(ecls_ready, 1)
                    highs(3)
                    copies(2, 3)

            steps(act, step)

        @block.vector
        def _(dve):
            V_ = nc.vector
            both = lambda ap: ap.rearrange("p (b t) -> p b t", b=2)

            def statistics(n, par, loads):
                dve.wait_ge(x_loaded[par], 16 * loads)
                for h in range(2):
                    last = V_.bn_stats(stats[:, h, :], xt[par][:, 512 * h:512 * h + 512])
                last.then_inc(stats_ready, 1)
                dve.wait_ge(stats_ready, n + 1)
                need(dve, xn_ready, n)
                hold(dve, passed_vector)
                V_.bn_aggr(mv[:], stats[:]).then_inc(mv_ready, 1)
                dve.wait_ge(mv_ready, n + 1)
                V_.tensor_scalar(mv[:, 1:2], mv[:, 1:2], EPS_LN, None, ALU.add).then_inc(var_eps, 1)

            def normalized(n, par, g_last):
                need(dve, item_ready, g_last + 1)
                dve.wait_ge(rstd_ready, n + 1)
                V_.tensor_scalar(xn[:], xt[par][:], mv[:, 0:1], rstd[:], ALU.subtract, ALU.mult).then_inc(xn_ready, 1)

            def take_rows(item, half, par, n):
                b, q = max(item[1], 0) % 2, item[2]
                dve.wait_ge(high_ready, n + 1)
                hi = xh[par][:, 2 * q:2 * q + 2, b * T:(b + 1) * T].bitcast(F32)
                V_.tensor_tensor(xl[par][:, 2 * q:2 * q + 2, b * T:(b + 1) * T],
                                 pI[half].rearrange("p (i t) -> p i t", i=2), hi,
                                 ALU.subtract).then_inc(item_taken, 1)

            def take(item, g, half, pair, r, par, buf):
                src = pI[half]
                dve.wait_ge(item_ready, g + 1)
                if item[0] == "v":
                    V_.tensor_tensor(V[par][:, item[1], :], src, vrow[:], ALU.subtract).then_inc(item_taken, 1)
                    return
                need(dve, roped, r - 1)
                cos = rope[:, 0:1, :].broadcast_to([P, 2, T])
                V_.tensor_tensor(both(rc[buf][:]), both(src), cos, ALU.mult)
                V_.stream_shuffle(rs[buf][:], src, [(i + HD // 2) % HD for i in range(HD)]).then_inc(item_taken, 1)
                if item[0] == "k":
                    dve.wait_ge(item_taken, g + 1)
                    V_.tensor_scalar(rc[buf][:], rc[buf][:], kcls[:, item[1]:item[1] + 1], None,
                                     ALU.subtract).then_inc(key_ready, 1)

            def mask_scores(s, j, par):
                dve.wait_ge(scored, 4 * s + j + 1)
                if j == 3:
                    need(dve, pt_ready, 4 * (s - 1))
                heads = lambda ap: ap.rearrange("p (m k) -> p m k", m=4)
                v = heads(pr[par][:, 4 * T * j:4 * T * (j + 1)])
                V_.tensor_tensor(v, heads(pS[j][:]), mask[:].unsqueeze(1).broadcast_to([P, 4, T]),
                                 ALU.add).then_inc(masked, 1)
                dve.wait_ge(masked, 4 * s + j + 1)
                V_.tensor_reduce(mx[par][:, 4 * j:4 * j + 4], v, AX.X, ALU.max).then_inc(maxed, 1)
                dve.wait_ge(maxed, 4 * s + j + 1)
                V_.tensor_scalar(nm[par][:, 4 * j:4 * j + 4], mx[par][:, 4 * j:4 * j + 4], -SCALE, 0.0,
                                 ALU.mult, ALU.min).then_inc(bias_ready, 1)

            def reciprocals(s, par):
                dve.wait_ge(exped, 4 * s + 4)
                dve.wait_ge(ecls_ready, s + 1)
                V_.tensor_tensor(sums[par][:], sums[par][:], ecls[par][:], ALU.add).then_inc(summed, 1)
                dve.wait_ge(summed, s + 1)
                V_.reciprocal(rec[par][:], sums[par][:]).then_inc(rec_ready, 1)

            dve.wait_ge(const_loaded, 48)
            rows_par = lambda item: 1 if item[1] < 0 or item[1] > 1 else 0
            last_of = {item[1]: g for g, item in enumerate(FIRST) if item[0] == "x"}
            statistics(0, 1, 1)
            normalized(0, 1, -1)
            statistics(1, 0, 1)
            r = n = 0
            for g, item in enumerate(FIRST):
                if item[0] == "x":
                    take_rows(item, g % 2, rows_par(item), n)
                    n += 1
                    if item[2] == 3:
                        tile = item[1] + 2
                        normalized(tile, (tile - 1) % 2, g)
                        if tile < LAG + 1:
                            statistics(tile + 1, tile % 2, (tile + 1) // 2 + (1 if tile % 2 == 0 else 1))
                    continue
                dve.wait_ge(item_ready, g + 1)
                src = pI[g % 2][:, 0:4].rearrange("p (k t) -> p k t", k=2)[:, :, 0]
                if item[0] == "cv":
                    V_.tensor_copy(vrow[:], pI[g % 2]).then_inc(item_taken, 1)
                elif item[0] == "ck":
                    V_.tensor_copy(kcls[:], src).then_inc(item_taken, 1)
                elif item[0] == "cvt":
                    V_.tensor_copy(vcol[:], src).then_inc(item_taken, 1)
                    dve.wait_ge(item_taken, g + 1)
                    for kb in range(2):
                        V_.tensor_copy(ob[kb][:], vcol[:, kb:kb + 1].broadcast_to([P, 4 * T])).then_inc(o_ready, 1)
                else:
                    take(item, g, g % 2, 0, r, 0, r % 2)
                    r += item[0] != "v"

            def step(t, par, nxt, rows, norm):
                its = item_list(t, nxt, rows)
                r = [0]

                def takes(u, k):
                    for item, g, half in slot_items(its, u, k):
                        if item[0] == "x":
                            take_rows(item, half, par, 20 + 8 * t + 4 * item[1] + item[2])
                        else:
                            take(item, g, half, t + 1, 10 * (t + 1) + r[0], 1 - par, r[0] % 2)
                            r[0] += item[0] != "v"

                for u in range(4):
                    s = 4 * t + u
                    q = (u + 1) % 2
                    soft = lambda *js: [mask_scores(s - 1, j, q) for j in js if is_unit(s - 1)]
                    soft(0, 1)
                    takes(u, 0)
                    soft(2)
                    if is_unit(s - 3):
                        take_output(s - 3, *earlier(t, u, 3))
                    takes(u, 1)
                    takes(u, 2)
                    soft(3)
                    takes(u, 3)
                    if is_unit(s - 1):
                        reciprocals(s - 1, q)
                    takes(u, 4)
                    b = norms_batch(t, u)
                    if norm and exists(b):
                        bpar = (u // 2 + LAG + 1) % 2
                        if u % 2 == 0:
                            statistics(b + 1, bpar, loads(b, u, t))
                        else:
                            g_last = [g for item, g, _ in slot_items(its, u, 3) if item[0] == "x"]
                            normalized(b + 1, bpar, g_last[0])

            def loads(b, u, t):
                return t + (LAG + 1 + u // 2) // 2 + 1 + (1 if (u // 2 + LAG + 1) % 2 == 1 else 0)

            def take_output(s, t, u):
                dve.wait_ge(pv_done, 4 * s + 4)
                dve.wait_ge(o_stored[u % 2], 16 * (2 * t + u // 2 + 1))
                V_.tensor_scalar(ob[u % 2][:], pO[:], vcol[:, u % 2:u % 2 + 1], None, ALU.add).then_inc(o_ready, 1)

            steps(dve, step)

        @block.tensor
        def _(pe):
            pe.wait_ge(const_loaded, 48)

            def three(out, lhs, rhs):
                n = 3 * IC
                for i in range(IC):
                    for k, (a, b) in enumerate(((0, 0), (0, 1), (1, 0))):
                        last = nc.tensor.matmul(out, lhs(a, i), rhs(b, i), start=(i == 0 and k == 0),
                                                stop=(i == IC - 1 and k == 2))
                return last

            def product(item, g, half, par, all_taken=False):
                need(pe, item_taken, g if all_taken else g - 1)
                out = pI[half]
                X = (xh[par], xl[par])
                W = (wh, wl)
                if item[0] == "x":
                    b, q = max(item[1], 0) % 2, item[2]
                    for i in range(2):
                        last = nc.tensor.transpose(out[:, i * T:(i + 1) * T],
                                                   xn[:, (2 * q + i) * P:(2 * q + i + 1) * P], ident[:])
                elif item[0] == "q":
                    last = three(out, lambda k, i: W[k][:, i, item[1] * P:(item[1] + 1) * P],
                                 lambda k, i: X[k][:, i, :])
                elif item[0] == "k":
                    c = D + item[1] * P
                    last = three(out, lambda k, i: W[k][:, i, c:c + P], lambda k, i: X[k][:, i, :])
                elif item[0] in ("v", "cv"):
                    b = item[1] if item[0] == "v" else 0
                    last = three(out, lambda k, i: X[k][:, i, b * T:(b + 1) * T],
                                 lambda k, i: W[k][:, i, D + KVW:D + 2 * KVW])
                else:
                    for kb in range(2):
                        c = D + kb * P + (KVW if item[0] == "cvt" else 0)
                        last = three(out[:, 2 * kb:2 * kb + 2], lambda k, i: W[k][:, i, c:c + P],
                                     lambda k, i: X[k][:, i, 0:2])
                last.then_inc(item_ready, 1)

            def scores(s, u, par):
                b, kb = u // 2, u % 2
                for m in range(4):
                    for j in range(4):
                        rows = slice(HD * j, HD * (j + 1))
                        if m == 0:
                            need(pe, masked, 4 * s + j - 3)
                        last = nc.tensor.matmul(pS[j][:, m * T:(m + 1) * T],
                                                QT[par][rows, 4 * kb + m, b * T:(b + 1) * T],
                                                KT[par][rows, kb, b * T:(b + 1) * T], start=True, stop=True)
                        if m == 3:
                            last.then_inc(scored, 1)

            def transposed(s, j, par):
                pe.wait_ge(normed, 4 * s + j + 1)
                need(pe, pt_copied, 4 * s + j)
                for m in range(4):
                    i = 4 * j + m
                    last = nc.tensor.transpose(pT[:, m * T:(m + 1) * T], pr[par][:, i * T:(i + 1) * T], ident[:])
                last.then_inc(pt_ready, 1)

            def weighted(s, j, u, par):
                b, kb = u // 2, u % 2
                pe.wait_ge(pt_copied, 4 * s + j + 1)
                if j == 0:
                    need(pe, o_ready, s + 2)
                c = HD * (4 * kb + j)
                nc.tensor.matmul(pO[HD * j:HD * (j + 1), :], V[par][:, b, c:c + HD], pt[j % 2][:],
                                 start=True, stop=True).then_inc(pv_done, 1)

            for g, item in enumerate(FIRST):
                if item[0] == "x":
                    pe.wait_ge(xn_ready, item[1] + 2)
                    product(item, g, g % 2, 1 if item[1] < 0 or item[1] > 1 else 0)
                else:
                    fresh = FIRST[g - 1][0] == "x"
                    product(item, g, g % 2, 1 if item[0][0] == "c" else 0, all_taken=fresh)

            def step(t, par, nxt, rows, norm):
                its = item_list(t, nxt, rows)

                def products(u, k):
                    for item, g, half in slot_items(its, u, k):
                        if item[0] == "x":
                            pe.wait_ge(xn_ready, 2 * t + LAG + item[1] + 2)
                            product(item, g, half, par)
                        else:
                            product(item, g, half, 1 - par, all_taken=isinstance(g, int) and g == NFIRST)

                for u in range(4):
                    s = 4 * t + u
                    w = earlier(t, u, 2)
                    tr = lambda j: transposed(s - 2, j, u % 2) if is_unit(s - 2) else None
                    wt = lambda j: weighted(s - 2, j, w[1], par if u >= 2 else 1 - par) if is_unit(s - 2) else None
                    products(u, 0)
                    if is_unit(s - 3):
                        weighted(s - 3, 3, earlier(t, u, 3)[1], par if u >= 3 else 1 - par)
                    tr(0)
                    products(u, 1)
                    products(u, 2)
                    wt(0)
                    tr(1)
                    products(u, 3)
                    products(u, 4)
                    wt(1)
                    tr(2)
                    if is_unit(s):
                        if u < 2:
                            pe.wait_ge(roped, 10 * t + (5 if u == 0 else 10))
                        scores(s, u, par)
                    wt(2)
                    tr(3)

            steps(pe, step)


def feed_forward(nc, mem, io):
    TILES = NB + 1
    HALF = D // 2
    with ExitStack() as ctx:
        sb = lambda n, s, d=F32: ctx.enter_context(nc.sbuf_tensor(n, s, d))
        sem = lambda n: ctx.enter_context(nc.semaphore(n))
        mem["wfl"] = sb("g_wfl", [P, IC * D], F32R)[:]
        ident = sb("g_ident", [P, P])
        at = [sb(f"g_at{i}", [P, D]) for i in range(2)]
        x = [sb(f"g_x{i}", [P, D]) for i in range(2)]
        ah = sb("g_ah", [P, IC, T], F32R)
        al = sb("g_al", [P, IC, T], F32R)
        h2 = [sb(f"g_h{i}", [P, D]) for i in range(3)]
        xn = sb("g_xn", [P, D])
        xh = sb("g_xh", [P, IC, T], F32R)
        xl = sb("g_xl", [P, IC, T], F32R)
        stats = sb("g_stats", [P, 2, 6])
        mv = sb("g_mv", [P, 2])
        rstd = sb("g_rstd", [P, 1])
        minus_half = sb("g_minus_half", [P, 1])
        pP = ctx.enter_context(nc.psum_tensor("g_pP", [P, D], F32))
        pX = ctx.enter_context(nc.psum_tensor("g_pX", [P, D], F32))
        pF = ctx.enter_context(nc.psum_tensor("g_pF", [P, D], F32))
        woh, wol, wfh, wfl = (mem[k].rearrange("p (i n) -> p i n", i=IC) for k in ("woh", "wol", "wfh", "wfl"))
        const_loaded = sem("g_const_loaded")
        wfl_loaded = sem("g_wfl_loaded")
        at_loaded = [sem(f"g_at_loaded{i}") for i in range(2)]
        x_loaded = [sem(f"g_x_loaded{i}") for i in range(2)]
        stored = [sem(f"g_stored{i}") for i in range(3)]
        half_ready = sem("g_half_ready")
        ah_ready = sem("g_ah_ready")
        al_ready = sem("g_al_ready")
        projected = sem("g_projected")
        h_ready = sem("g_h_ready")
        stats_ready = sem("g_stats_ready")
        mv_ready = sem("g_mv_ready")
        var_eps = sem("g_var_eps_ready")
        rstd_ready = sem("g_rstd_ready")
        xn_ready = sem("g_xn_ready")
        transposed = sem("g_transposed")
        xh_ready = sem("g_xh_ready")
        xl_ready = sem("g_xl_ready")
        fed = sem("g_fed")
        y_ready = sem("g_y_ready")
        passed_vector = sem("g_passed_vector")
        block = ctx.enter_context(nc.Block())
        U = 6

        def tiles(engine, step):
            for u in range(U):
                step(u, u, 0)
            with engine.Fori(1, TILES // U) as i:
                for u in range(U):
                    step(U * i + u, u, i)
            done = TILES // U * U
            for b in range(done, TILES):
                step(b, b % U, b // U)

        def loads_of(u, i):
            return U // 2 * i + u // 2 + 1

        @block.sync
        def _(sp):
            sp.dma_start(ident[:], io["ident"]).then_inc(const_loaded, 16)

            def load(b, u):
                need(sp, al_ready, b - 1)
                src = io["attn"][bass.ds(b, 1)].rearrange("o p n -> (o p) n")
                sp.dma_start(at[u % 2][:], src).then_inc(at_loaded[u % 2], 16)
                need(sp, h_ready, 2 * (b - 1))
                src = io["x_tok"][bass.ds(b, 1)].rearrange("o t d -> (o t) d")
                sp.dma_start(x[u % 2][:], src).then_inc(x_loaded[u % 2], 16)

            load(0, 0)
            load(1, 1)
            sp.dma_start(wfl.bitcast(F32), io["wfl"]).then_inc(wfl_loaded, 16)

            def step(b, u, i):
                if not (isinstance(b, int) and b + 2 >= TILES):
                    load(b + 2, u)
                sp.wait_ge(y_ready, 2 * (b + 1))
                if isinstance(b, int) and b == NB:
                    sp.dma_start(io["out"][:, 0, :], h2[u % 3][0:NB, :]).then_inc(stored[u % 3], 16)
                else:
                    dst = io["out"][bass.ds(b, 1), 1:T + 1, :].rearrange("o t d -> (o t) d")
                    sp.dma_start(dst, h2[u % 3][:]).then_inc(stored[u % 3], 16)

            tiles(sp, step)
            for k in range(3):
                sp.wait_ge(stored[k], 16 * (TILES // 3))

        @block.gpsimd
        def _(pool):
            nc.gpsimd.memset(minus_half[:], -0.5).then_inc(half_ready, 1)
            pool.wait_ge(half_ready, 1)

            def step(b, u, i):
                pool.wait_ge(var_eps, b + 1)
                nc.gpsimd.tensor_tensor(rstd[:], mv[:, 1:2], minus_half[:], ALU.pow).then_inc(rstd_ready, 1)

            tiles(pool, step)

        @block.scalar
        def _(act):
            def high_attn(b, u, loads):
                act.wait_ge(at_loaded[u % 2], 16 * loads)
                need(act, projected, 2 * b)
                nc.scalar.activation(ah[:].rearrange("p i t -> p (i t)"), at[u % 2][:], ACT.Copy).then_inc(ah_ready, 1)

            high_attn(0, 0, 1)
            high_attn(1, 1, 1)

            def step(b, u, i):
                for h in range(2):
                    act.wait_ge(transposed, 2 * b + h + 1)
                    need(act, fed, 2 * b)
                    nc.scalar.activation(xh[:, 4 * h:4 * h + 4, :], pX[:, HALF * h:HALF * (h + 1)].rearrange(
                        "p (i t) -> p i t", i=4), ACT.Copy).then_inc(xh_ready, 1)
                if not (isinstance(b, int) and b + 2 >= TILES):
                    high_attn(b + 2, u, loads_of(u + 2, i))

            tiles(act, step)

        @block.vector
        def _(dve):
            V_ = nc.vector

            def low_attn(b, u):
                dve.wait_ge(ah_ready, b + 1)
                V_.tensor_tensor(al[:].rearrange("p i t -> p (i t)"), at[u % 2][:],
                                 ah[:].rearrange("p i t -> p (i t)").bitcast(F32), ALU.subtract).then_inc(al_ready, 1)

            def residual_and_norm(b, u, i):
                dve.wait_ge(x_loaded[u % 2], 16 * loads_of(u, i))
                need(dve, stored[u % 3], 16 * (2 * i + u // 3))
                hb = h2[u % 3]
                for h in range(2):
                    cols = slice(HALF * h, HALF * (h + 1))
                    dve.wait_ge(projected, 2 * b + h + 1)
                    V_.tensor_tensor(hb[:, cols], pP[:, cols], x[u % 2][:, cols], ALU.add).then_inc(h_ready, 1)
                for h in range(2):
                    dve.wait_ge(h_ready, 2 * b + h + 1)
                    last = V_.bn_stats(stats[:, h, :], hb[:, HALF * h:HALF * (h + 1)])
                last.then_inc(stats_ready, 1)
                dve.wait_ge(stats_ready, b + 1)
                need(dve, xn_ready, b)
                hold(dve, passed_vector)
                V_.bn_aggr(mv[:], stats[:]).then_inc(mv_ready, 1)
                dve.wait_ge(mv_ready, b + 1)
                V_.tensor_scalar(mv[:, 1:2], mv[:, 1:2], EPS_LN, None, ALU.add).then_inc(var_eps, 1)
                dve.wait_ge(rstd_ready, b + 1)
                need(dve, transposed, 2 * b)
                V_.tensor_scalar(xn[:], hb[:], mv[:, 0:1], rstd[:], ALU.subtract, ALU.mult).then_inc(xn_ready, 1)

            low_attn(0, 0)
            residual_and_norm(0, 0, 0)
            low_attn(1, 1)

            def step(b, u, i):
                for h in range(2):
                    dve.wait_ge(xh_ready, 2 * b + h + 1)
                    V_.tensor_tensor(xl[:, 4 * h:4 * h + 4, :],
                                     pX[:, HALF * h:HALF * (h + 1)].rearrange("p (i t) -> p i t", i=4),
                                     xh[:, 4 * h:4 * h + 4, :].bitcast(F32), ALU.subtract).then_inc(xl_ready, 1)
                if not (isinstance(b, int) and b + 1 >= TILES):
                    residual_and_norm(b + 1, u + 1, i)
                if not (isinstance(b, int) and b + 2 >= TILES):
                    low_attn(b + 2, u)
                for h in range(2):
                    cols = slice(HALF * h, HALF * (h + 1))
                    dve.wait_ge(fed, 2 * b + h + 1)
                    V_.tensor_tensor(h2[u % 3][:, cols], pF[:, cols], h2[u % 3][:, cols], ALU.add).then_inc(y_ready, 1)

            tiles(dve, step)

        @block.tensor
        def _(pe):
            pe.wait_ge(const_loaded, 16)
            pe.wait_ge(mem["parts_loaded"], 48)

            def three(out, parts, weights, h, done):
                cols = slice(HALF * h, HALF * (h + 1))
                for i in range(IC):
                    for k, (a, b) in enumerate(((0, 0), (0, 1), (1, 0))):
                        last = nc.tensor.matmul(out[:, cols], parts[a][:, i, :], weights[b][:, i, cols],
                                                start=(i == 0 and k == 0), stop=(i == IC - 1 and k == 2))
                last.then_inc(done, 1)

            def project(b):
                pe.wait_ge(al_ready, b + 1)
                need(pe, h_ready, 2 * b)
                for h in range(2):
                    three(pP, (ah, al), (woh, wol), h, projected)

            project(0)

            def step(b, u, i):
                pe.wait_ge(xn_ready, b + 1)
                need(pe, xl_ready, 2 * b)
                for h in range(2):
                    for q in range(4 * h, 4 * h + 4):
                        last = nc.tensor.transpose(pX[:, q * T:(q + 1) * T], xn[:, q * P:(q + 1) * P], ident[:])
                    last.then_inc(transposed, 1)
                if not (isinstance(b, int) and b + 1 >= TILES):
                    project(b + 1)
                pe.wait_ge(xl_ready, 2 * b + 2)
                if isinstance(b, int) and b == 0:
                    pe.wait_ge(wfl_loaded, 16)
                need(pe, y_ready, 2 * b)
                for h in range(2):
                    three(pF, (xh, xl), (wfh, wfl), h, fed)

            tiles(pe, step)


def build(nc, io):
    with ExitStack() as ctx:
        keep = lambda c, n, s, d=F32: c.enter_context(nc.sbuf_tensor(n, s, d))[:]
        io["x_tok"] = nc.dram_tensor("x_tok", [NB + 1, T, D], F32, kind="Internal").ap()
        io["attn"] = nc.dram_tensor("attn", [NB + 1, P, D], F32, kind="Internal").ap()
        for name in ("woh", "wol", "wfh", "wfl"):
            io[name] = nc.dram_tensor(name, [P, IC, D], F32, kind="Internal").ap()
        mem = {}
        mem["parts_loaded"] = ctx.enter_context(nc.semaphore("parts_loaded"))
        with ExitStack() as tabs:
            segs, at = {}, 0
            for name, n in (("C1", P * NC), ("C2", P * NC), ("D1", P * ND), ("D2", P * ND),
                            ("Ar", P * NA), ("Ai", P * NA), ("Y", 4 * P), ("end", 0)):
                segs[name] = (at, n)
                at += n
            mem["segs"] = segs
            mem["w_loaded"] = tabs.enter_context(nc.semaphore("w_loaded"))
            mem["w1"] = keep(tabs, "w1", [P, P * NB])
            mem["w2"] = keep(tabs, "w2", [P, P * NB])
            mem["trig"] = keep(tabs, "trig", [P, at])
            mem["FA"] = keep(tabs, "FA", [P, 2, P * NA])
            position_tables(nc, mem, io)
            W = IC * QKV
            region = ctx.enter_context(nc.sbuf_tensor("weights", [P, 2 * W], F32R, side="right"))
            mem["wh"], mem["wl"] = region[:, 0:W], region[:, W:2 * W]
            for i, name in enumerate(("woh", "wol", "wfh")):
                mem[name] = region[:, IC * D * i:IC * D * (i + 1)]
            token_kernels(nc, mem, io)
        attention(nc, mem, io)
        feed_forward(nc, mem, io)


def kernel(x, cls_tok, L0_tok_log_dt, L0_tok_Lambda, L0_attn_wq, L0_attn_wk, L0_attn_wv, L0_attn_wo,
           L0_ffn_bases, L0_ffn_alphas):
    import concourse.bacc as bacc
    from concourse.bass_utils import run_bass_kernel_spmd

    lay = np.ascontiguousarray
    f = lambda a: np.asarray(a)
    heads = lambda w: w.reshape(2, 4, GROUPS, HD, -1).transpose(0, 2, 1, 3, 4).reshape(D, -1)
    wq, wk, wv, wo = f(L0_attn_wq), f(L0_attn_wk), f(L0_attn_wv), f(L0_attn_wo)
    chunks = lambda w: lay(w.reshape(IC, P, -1).transpose(1, 0, 2))
    arrays = {
        "W": lay(f(x).transpose(3, 2, 1, 0)).reshape(P, P * NB),
        "log_dt": lay(f(L0_tok_log_dt).T),
        "Lambda": lay(f(L0_tok_Lambda)),
        "cls": lay(f(cls_tok).reshape(D)),
        "wqkv": chunks(np.concatenate([heads(wq).T, wk.T, wv.T], axis=1)).reshape(P, P // 4, -1),
        "wo": chunks(heads(lay(wo.T))),
        "bases": lay(f(L0_ffn_bases).reshape(4, IC, P, D).transpose(2, 1, 0, 3)),
        "alphas": lay(f(L0_ffn_alphas).reshape(4, IC, P).transpose(2, 1, 0)).reshape(P, -1),
    }
    arrays.update(host_constants())
    nc = bacc.Bacc("TRN2", target_bir_lowering=False, num_devices=1)
    io = {}
    for name, a in arrays.items():
        io[name] = nc.dram_tensor("in_" + name, a.shape, mybir.dt.from_np(a.dtype), kind="ExternalInput").ap()
    io["out"] = nc.dram_tensor("out_tokens", (NB, T + 1, D), F32, kind="ExternalOutput").ap()
    build(nc, io)
    r = run_bass_kernel_spmd(nc, [{"in_" + k: a for k, a in arrays.items()}], core_ids=[0])
    return r.results[0]["out_tokens"]
```
